# Optimizing a Trainium2 kernel written in Bass

```python
import numpy as np
import jax
import jax.numpy as jnp

def _softmax(x, axis=-1):
    return jax.nn.softmax(x, axis=axis)

def _gelu(x):
    return jax.nn.gelu(x, approximate=True)

def _silu(x):
    return jax.nn.silu(x)

def _sigmoid(x):
    return jax.nn.sigmoid(x)

def _layernorm(x, axis=-1, eps=1e-05):
    m = jnp.mean(x, axis=axis, keepdims=True)
    v = jnp.var(x, axis=axis, keepdims=True)
    return (x - m) / jnp.sqrt(v + eps)

def _scatter_add(tgt, idx, src, axis=0):
    return tgt.at[idx].add(src)

def _segment_sum(src, seg, n):
    return jax.ops.segment_sum(src, seg, n)
kernel_name = 'mk_adaln_ffn_d1_seqx_r4_780567'

def setup_inputs(seed: int=0):
    np.random.seed(seed)
    _w = jnp.asarray

    def _rec_inputs():
        import jax
        import jax.numpy as jnp
        _rk = jax.random.key(seed)
        x = -0.000125 + 0.9999 * jax.random.normal(jax.random.fold_in(_rk, 1), (16, 256, 256), jnp.float32)
        _lenS = 256 - jax.random.randint(jax.random.fold_in(_rk, 7), (16,), 0, max(1, 256 // 4) + 1, jnp.int32)
        _lenS2 = 256 - jax.random.randint(jax.random.fold_in(_rk, 8), (16,), 0, max(1, 256 // 4) + 1, jnp.int32)
        cond_1024 = 0.00513981 + 1.0024 * jax.random.normal(jax.random.fold_in(_rk, 11), (16, 256), jnp.float32)
        return (x, cond_1024)
    x, cond_1024 = _rec_inputs()

    def _L0_cond_setup():
        import jax, jax.numpy as jnp
        import numpy as np
        IN_FEATURES = 256
        OUT_FEATURES = 256
        BATCH = 32
        SEQ = 256
        EPS = 1e-08
        key = jax.random.key(seed)
        k1, k2, k3 = jax.random.split(key, 3)
        Efou = jax.random.normal(k1, (BATCH, SEQ, IN_FEATURES), dtype=jnp.float32)
        y = jax.random.normal(k2, (BATCH, IN_FEATURES), dtype=jnp.float32)
        weight = jax.random.normal(k3, (IN_FEATURES, OUT_FEATURES), dtype=jnp.float32)
        return {'Efou': Efou, 'y': y, 'weight': weight}
    _L0_cond_all = _L0_cond_setup()
    _L0_cond_in = {k: v for k, v in _L0_cond_all.items() if k in ('weight',)}
    del _L0_cond_all

    def _L0_ffn_setup():
        import jax, jax.numpy as jnp
        import numpy as np
        import math
        D_IN = 256
        FEATURES = (1024, 1024, 256)
        BATCH, SEQ = (8, 512)

        def _conn_dense(kernel_bool, x):
            w = jnp.where(kernel_bool, jnp.float32(1.0), jnp.float32(-1.0))
            return x @ w
        key = jax.random.key(seed)
        kx, kk0, kk1, kk2 = jax.random.split(key, 4)
        x = jax.random.normal(kx, (BATCH, SEQ, D_IN), dtype=jnp.float32)
        k0 = jax.random.randint(kk0, (2 * D_IN, FEATURES[0]), 0, 2).astype(jnp.bool_)
        k1 = jax.random.randint(kk1, (FEATURES[0], FEATURES[1]), 0, 2).astype(jnp.bool_)
        k2 = jax.random.randint(kk2, (FEATURES[1], FEATURES[2]), 0, 2).astype(jnp.bool_)
        s0 = jnp.asarray(1.0 / math.sqrt(2 * D_IN), dtype=jnp.float32)
        s1 = jnp.asarray(1.0 / math.sqrt(FEATURES[0]), dtype=jnp.float32)
        s2 = jnp.asarray(1.0 / math.sqrt(FEATURES[1]), dtype=jnp.float32)
        return {'x': x, 'k0': k0, 'k1': k1, 'k2': k2, 's0': s0, 's1': s1, 's2': s2}
    _L0_ffn_all = _L0_ffn_setup()
    _L0_ffn_in = {k: v for k, v in _L0_ffn_all.items() if k in ('k0', 'k1', 'k2', 's0', 's1', 's2')}
    del _L0_ffn_all
    return {'x': x, 'cond_1024': cond_1024, 'L0_cond_weight': _L0_cond_in['weight'], 'L0_ffn_k0': _L0_ffn_in['k0'], 'L0_ffn_k1': _L0_ffn_in['k1'], 'L0_ffn_k2': _L0_ffn_in['k2'], 'L0_ffn_s0': _L0_ffn_in['s0'], 'L0_ffn_s1': _L0_ffn_in['s1'], 'L0_ffn_s2': _L0_ffn_in['s2']}

def reference(x, cond_1024, L0_cond_weight, L0_ffn_k0, L0_ffn_k1, L0_ffn_k2, L0_ffn_s0, L0_ffn_s1, L0_ffn_s2):
    import jax
    import jax.numpy as jnp

    def _L0_cond_ref(Efou, y, weight):
        import jax, jax.numpy as jnp
        import numpy as np
        IN_FEATURES = 256
        OUT_FEATURES = 256
        BATCH = 32
        SEQ = 256
        EPS = 1e-08
        scale = 1.0 / np.sqrt(np.float32(weight.shape[0]))
        ys = y * scale
        d = jax.lax.rsqrt(jnp.einsum('bi,io->bo', ys * ys, weight * weight) + EPS)
        out = jnp.einsum('bsi,io->bso', Efou * ys[:, None, :], weight) * d[:, None, :]
        return out

    def _L0_ffn_ref(x, k0, k1, k2, s0, s1, s2):
        import jax, jax.numpy as jnp
        import numpy as np
        import math
        D_IN = 256
        FEATURES = (1024, 1024, 256)
        BATCH, SEQ = (8, 512)

        def _conn_dense(kernel_bool, x):
            w = jnp.where(kernel_bool, jnp.float32(1.0), jnp.float32(-1.0))
            return x @ w
        h = jnp.concatenate([x, -x], axis=-1)
        h = s0 * _conn_dense(k0, h)
        h = jax.nn.relu(h) * 2
        h = s1 * _conn_dense(k1, h)
        h = jax.nn.relu(h) * 2
        h = s2 * _conn_dense(k2, h)
        return h
    x = x + _L0_ffn_ref(_L0_cond_ref(x, cond_1024, L0_cond_weight), L0_ffn_k0, L0_ffn_k1, L0_ffn_k2, L0_ffn_s0, L0_ffn_s1, L0_ffn_s2)
    return x

_drawn_inputs = setup_inputs


def setup_inputs(seed=0):
    import zlib

    import numpy as np

    out = dict(_drawn_inputs(seed))
    spreads = {}
    factors = {}
    for name, (base, spread) in spreads.items():
        noise = np.random.default_rng([zlib.crc32(name.encode()), seed]).standard_normal(out[name].shape)
        drawn = base * np.exp(spread * noise) if base else spread * noise
        out[name] = jnp.asarray(drawn.astype(out[name].dtype))
    for name, factor in factors.items():
        out[name] = (out[name] * factor).astype(out[name].dtype)
    return out
```

```python
import concourse.bass as bass
from concourse import mybir
from contextlib import ExitStack

P = 128
BATCH, SEQ, D = 16, 256, 256
HID = 1024
EPS = 1e-8
ROWS = 512
CHUNKS = BATCH * SEQ // ROWS
PER = ROWS // SEQ
KD, KH = D // P, HID // P
RING = 4
WIDE = 2 * KH


def build(nc, x, cond, w, k0, k1, k2, s, out):
    fp32, fp32r, u8 = mybir.dt.float32, mybir.dt.float32r, mybir.dt.uint8
    ALU = mybir.AluOpType
    ACT = mybir.ActivationFunctionType

    ctx = ExitStack()
    with ctx:
        def sb(name, shape, dt=fp32):
            return ctx.enter_context(nc.sbuf_tensor(name, shape, dt))

        def banks(name, n):
            return [ctx.enter_context(nc.psum_tensor(f"{name}{i}", [P, ROWS], fp32)) for i in range(n)]

        def sem(name):
            return ctx.enter_context(nc.semaphore(name))

        x_sb = sb("x_sb", [P, CHUNKS, KD, ROWS])
        cond_sb = sb("cond_sb", [P, KD, BATCH])
        w_sb = sb("w_sb", [P, KD, D])
        s_sb = sb("s_sb", [P, 3])
        k0_sb = sb("k0_sb", [P, KH, 2, KD, P], u8)
        k1_sb = sb("k1_sb", [P, KH, KH, P], u8)
        k2_sb = sb("k2_sb", [P, KH, D], u8)
        ys = sb("ys", [P, KD, BATCH])
        ys2 = sb("ys2", [P, KD, BATCH])
        w2_sb = sb("w2_sb", [P, KD, D])
        var = sb("var", [P, KD, BATCH])
        root = sb("root", [P, KD, BATCH])
        rough = sb("rough", [P, KD, BATCH])
        step_a = sb("step_a", [P, KD, BATCH])
        step_b = sb("step_b", [P, KD, BATCH])
        demod = sb("demod", [P, KD, BATCH])
        gain = sb("gain", [P, 2])
        wt0 = sb("wt0", [P, KH, KD, P], fp32r)
        wt1 = sb("wt1", [P, KH, KH, P], fp32r)
        wt2 = sb("wt2", [P, KH, D], fp32r)
        xs = sb("xs", [P, KD, ROWS])
        h0 = [sb(f"h0_{part}", [P, KD, ROWS], fp32r) for part in ("hi", "lo")]
        h1 = [sb(f"h1_{part}", [P, KH, ROWS], fp32r) for part in ("hi", "lo")]
        h2 = [sb(f"h2_{part}", [P, KH, ROWS], fp32r) for part in ("hi", "lo")]
        t_cond = sb("t_cond", [P, KD, ROWS])
        t_wide = sb("t_wide", [P, RING, ROWS])

        wide_ps = banks("wide_ps", RING)
        cond_ps = banks("cond_ps", KD)
        out_ps = banks("out_ps", KD)

        cond_in, w_in, s_in = sem("cond_in"), sem("w_in"), sem("s_in")
        x_in = [sem(f"x_in{c}") for c in range(CHUNKS)]
        k0_in, k1_in, k2_in = [sem("k0_in0"), sem("k0_in1")], [sem("k1_in0"), sem("k1_in1")], sem("k2_in")
        ys_made, setup_v = sem("ys_made"), sem("setup_v")
        squares_made = sem("squares_made")
        var_summed, var_made, root_made, demod_made = (
            sem("var_summed"), sem("var_made"), sem("root_made"), sem("demod_made"))
        gain_made = sem("gain_made")
        wt0_made, wt1_made, wt2_made = sem("wt0_made"), sem("wt1_made"), sem("wt2_made")
        xs_made = sem("xs_made")
        cond_done = sem("cond_done")
        cond_scaled = sem("cond_scaled")
        cond_split = sem("cond_split")
        wide_done = sem("wide_done")
        wide_relu = sem("wide_relu")
        wide_split = sem("wide_split")
        hi_made = sem("hi_made")
        out_done = sem("out_done")
        y_made = sem("y_made")
        y_stored = sem("y_stored")

        block = ctx.enter_context(nc.Block())

        @block.sync
        def _(sp):
            sp.dma_start(w_sb[:], w).then_inc(w_in, 16)
            sp.dma_start(x_sb[:, 0], x[:, 0]).then_inc(x_in[0], 16)
            half = KH // 2
            for i in range(2):
                sp.dma_start(k0_sb[:, i * half:(i + 1) * half], k0[:, i * half:(i + 1) * half]).then_inc(k0_in[i], 16)
            sp.dma_start(x_sb[:, 1], x[:, 1]).then_inc(x_in[1], 16)
            for i in range(2):
                sp.dma_start(k1_sb[:, i * half:(i + 1) * half], k1[:, i * half:(i + 1) * half]).then_inc(k1_in[i], 16)
            sp.dma_start(k2_sb[:], k2).then_inc(k2_in, 16)
            for c in range(2, CHUNKS):
                sp.dma_start(x_sb[:, c], x[:, c]).then_inc(x_in[c], 16)

            def store(c):
                for m in range(KD):
                    sp.wait_ge(y_made, KD * c + m + 1)
                    sp.dma_start(out[:, c, m], x_sb[:, c, m]).then_inc(y_stored, 16)

            with sp.Fori(0, CHUNKS) as c:
                store(c)
            sp.wait_ge(y_stored, 16 * KD * CHUNKS)

        @block.gpsimd
        def _(pool):
            for m in range(KH):
                if m % (KH // 2) == 0:
                    pool.wait_ge(k1_in[m // (KH // 2)], 16)
                pool.tensor_scalar(wt1[:, m], k1_sb[:, m], 2.0, -1.0, ALU.mult, ALU.add).then_inc(wt1_made, 1)
            pool.wait_ge(k2_in, 16)
            pool.tensor_scalar(wt2[:], k2_sb[:], 2.0, -1.0, ALU.mult, ALU.add).then_inc(wt2_made, 1)

        @block.scalar
        def _(act):
            act.dma_start(cond_sb[:], cond).then_inc(cond_in, 16)
            act.dma_start(s_sb[:], s.to_broadcast([P, 3])).then_inc(s_in, 16)

            def modulate(c, loaded):
                if loaded is not None:
                    act.wait_ge(loaded, 16)
                for kt in range(KD):
                    for b in range(PER):
                        last = act.activation(xs[:, kt, b * SEQ:(b + 1) * SEQ], x_sb[:, c, kt, b * SEQ:(b + 1) * SEQ],
                                              ACT.Copy, scale=ys[:, kt, bass.ds(PER * c + b, 1)])
                last.then_inc(xs_made, 1)

            def scale_cond(c, first=False):
                for m in range(KD):
                    act.wait_ge(cond_done, KD * c + m + 1)
                    if not first:
                        act.wait_ge(cond_split, KD * (c - 1) + m + 1)
                    for b in range(PER):
                        last = act.activation(t_cond[:, m, b * SEQ:(b + 1) * SEQ], cond_ps[m][:, b * SEQ:(b + 1) * SEQ],
                                              ACT.Copy, scale=demod[:, m, bass.ds(PER * c + b, 1)])
                    last.then_inc(cond_scaled, 1)

            def relu(c, layer, first=False):
                for m in range(KH):
                    n = WIDE * c + KH * layer + m
                    act.wait_ge(wide_done, n + 1)
                    if not (first and m < RING):
                        act.wait_ge(wide_split, n - RING + 1)
                    act.activation(t_wide[:, m % RING], wide_ps[m % RING][:], ACT.Relu,
                                   scale=gain[:, layer:layer + 1]).then_inc(wide_relu, 1)

            act.wait_ge(ys_made, 1)
            modulate(0, x_in[0])
            act.wait_ge(var_made, 1)
            act.activation(root[:], var[:], ACT.Sqrt).then_inc(root_made, 1)
            act.wait_ge(demod_made, 1)
            scale_cond(0, first=True)
            modulate(1, x_in[1])
            act.wait_ge(gain_made, 1)
            relu(0, 0, first=True)
            scale_cond(1)
            for c in range(2, CHUNKS):
                act.wait_ge(x_in[c], 16)
            modulate(2, None)
            relu(0, 1)
            with act.Fori(1, CHUNKS - 2) as c:
                relu(c, 0)
                scale_cond(c + 1)
                modulate(c + 2, None)
                relu(c, 1)
            relu(CHUNKS - 2, 0)
            scale_cond(CHUNKS - 1)
            relu(CHUNKS - 2, 1)
            relu(CHUNKS - 1, 0)
            relu(CHUNKS - 1, 1)

        @block.vector
        def _(dve):
            def split(t, h, slot, ready, count):
                dve.tensor_copy(h[0][:, slot], t).then_inc(hi_made, 1)
                dve.wait_ge(hi_made, count)
                dve.tensor_tensor(h[1][:, slot], t, h[0][:, slot].bitcast(fp32), ALU.subtract).then_inc(ready, 1)

            def before(c):
                return (WIDE + KD) * c + KD

            def split_cond(c, at):
                for m in range(KD):
                    dve.wait_ge(cond_scaled, KD * c + m + 1)
                    split(t_cond[:, m], h0, m, cond_split, at + m + 1)

            def split_wide(c, layer, at):
                for m in range(KH):
                    dve.wait_ge(wide_relu, WIDE * c + KH * layer + m + 1)
                    split(t_wide[:, m % RING], (h1, h2)[layer], m, wide_split, at + m + 1)

            def finish(c):
                for m in range(KD):
                    dve.wait_ge(out_done, KD * c + m + 1)
                    dve.scalar_tensor_tensor(x_sb[:, c, m], out_ps[m][:], s_sb[:, 2:3], x_sb[:, c, m],
                                             ALU.mult, ALU.add).then_inc(y_made, 1)

            dve.wait_ge(cond_in, 16)
            dve.tensor_scalar(ys[:], cond_sb[:], float(D) ** -0.5, None, ALU.mult).then_inc(ys_made, 1)
            dve.wait_ge(ys_made, 1)
            dve.tensor_tensor(ys2[:], ys[:], ys[:], ALU.mult).then_inc(squares_made, 1)
            dve.wait_ge(w_in, 16)
            dve.tensor_tensor(w2_sb[:], w_sb[:], w_sb[:], ALU.mult).then_inc(squares_made, 1)
            dve.wait_ge(s_in, 16)
            dve.tensor_scalar(gain[:, 0:1], s_sb[:, 0:1], 4.0, None, ALU.mult).then_inc(gain_made, 1)
            dve.tensor_scalar(gain[:, 1:2], s_sb[:, 1:2], 2.0, None, ALU.mult).then_inc(setup_v, 1)
            dve.wait_ge(var_summed, 1)
            for m in range(KD):
                last = dve.tensor_scalar(var[:, m], out_ps[m][:, 0:BATCH], EPS, None, ALU.add)
            last.then_inc(var_made, 1)
            dve.wait_ge(root_made, 1)
            dve.reciprocal(rough[:], root[:]).then_inc(setup_v, 1)
            dve.wait_ge(setup_v, 2)
            dve.scalar_tensor_tensor(step_a[:], rough[:], -0.5, var[:], ALU.mult, ALU.mult).then_inc(setup_v, 1)
            dve.wait_ge(setup_v, 3)
            dve.tensor_tensor(step_b[:], step_a[:], rough[:], ALU.mult).then_inc(setup_v, 1)
            dve.wait_ge(setup_v, 4)
            dve.scalar_tensor_tensor(demod[:], step_b[:], 1.5, rough[:], ALU.add, ALU.mult).then_inc(demod_made, 1)
            for m in range(KH):
                if m % (KH // 2) == 0:
                    dve.wait_ge(k0_in[m // (KH // 2)], 16)
                dve.tensor_tensor(wt0[:, m], k0_sb[:, m, 0], k0_sb[:, m, 1], ALU.subtract).then_inc(wt0_made, 1)

            split_cond(0, 0)
            split_wide(0, 0, before(0))
            split_cond(1, before(0) + KH)
            split_wide(0, 1, before(0) + KH + KD)
            with dve.Fori(1, CHUNKS - 1) as c:
                split_wide(c, 0, before(c))
                split_cond(c + 1, before(c) + KH)
                finish(c - 1)
                split_wide(c, 1, before(c) + KH + KD)
            c = CHUNKS - 1
            split_wide(c, 0, before(c))
            finish(c - 1)
            split_wide(c, 1, before(c) + KH)
            finish(c)

        @block.tensor
        def _(pe):
            def project(c, first=False):
                pe.wait_ge(xs_made, c + 1)
                for m in range(KD):
                    if not first:
                        pe.wait_ge(cond_scaled, KD * (c - 1) + m + 1)
                    for kt in range(KD):
                        mm = pe.matmul(cond_ps[m][:], w_sb[:, kt, m * P:(m + 1) * P], xs[:, kt],
                                       start=(kt == 0), stop=(kt == KD - 1))
                    mm.then_inc(cond_done, 1)

            def layer1(c, first=False):
                for m in range(KH):
                    n = WIDE * c + m
                    if first:
                        pe.wait_ge(wt0_made, m + 1)
                    if not (first and m < RING):
                        pe.wait_ge(wide_relu, n - RING + 1)
                    for kt in range(KD):
                        if m == 0:
                            pe.wait_ge(cond_split, KD * c + kt + 1)
                        for part in range(2):
                            mm = pe.matmul(wide_ps[m % RING][:], wt0[:, m, kt], h0[part][:, kt],
                                           start=(kt == 0 and part == 0), stop=(kt == KD - 1 and part == 1))
                    mm.then_inc(wide_done, 1)

            def layer2(c, first=False):
                for m in range(KH):
                    n = WIDE * c + KH + m
                    if first:
                        pe.wait_ge(wt1_made, m + 1)
                    pe.wait_ge(wide_relu, n - RING + 1)
                    for kt in range(KH):
                        if m == 0:
                            pe.wait_ge(wide_split, WIDE * c + kt + 1)
                        for part in range(2):
                            mm = pe.matmul(wide_ps[m % RING][:], wt1[:, m, kt], h1[part][:, kt],
                                           start=(kt == 0 and part == 0), stop=(kt == KH - 1 and part == 1))
                    mm.then_inc(wide_done, 1)

            def layer3(c, first=False):
                if first:
                    pe.wait_ge(wt2_made, 1)
                else:
                    pe.wait_ge(y_made, KD * c)
                for kt in range(KH):
                    pe.wait_ge(wide_split, WIDE * c + KH + kt + 1)
                    for m in range(KD):
                        for part in range(2):
                            mm = pe.matmul(out_ps[m][:], wt2[:, kt, m * P:(m + 1) * P], h2[part][:, kt],
                                           start=(kt == 0 and part == 0), stop=(kt == KH - 1 and part == 1))
                        if kt == KH - 1:
                            mm.then_inc(out_done, 1)

            pe.wait_ge(squares_made, 2)
            for m in range(KD):
                for kt in range(KD):
                    mm = pe.matmul(out_ps[m][:, 0:BATCH], w2_sb[:, kt, m * P:(m + 1) * P], ys2[:, kt],
                                   start=(kt == 0), stop=(kt == KD - 1))
            mm.then_inc(var_summed, 1)
            project(0, first=True)
            layer1(0, first=True)
            project(1)
            layer2(0, first=True)
            layer1(1)
            project(2)
            layer3(0, first=True)
            layer2(1)
            with pe.Fori(2, CHUNKS - 1) as c:
                layer1(c)
                project(c + 1)
                layer3(c - 1)
                layer2(c)
            layer1(CHUNKS - 1)
            layer3(CHUNKS - 2)
            layer2(CHUNKS - 1)
            layer3(CHUNKS - 1)


def kernel(x, cond_1024, L0_cond_weight, L0_ffn_k0, L0_ffn_k1, L0_ffn_k2, L0_ffn_s0, L0_ffn_s1, L0_ffn_s2):
    import numpy as np
    import concourse.bacc as bacc
    from concourse.bass_utils import run_bass_kernel_spmd

    arrays = {
        "x": np.asarray(x).reshape(CHUNKS, ROWS, KD, P).transpose(3, 0, 2, 1),
        "cond": np.asarray(cond_1024).reshape(BATCH, KD, P).transpose(2, 1, 0),
        "w": np.asarray(L0_cond_weight).reshape(KD, P, D).transpose(1, 0, 2),
        "k0": np.asarray(L0_ffn_k0).reshape(2, KD, P, KH, P).transpose(2, 3, 0, 1, 4),
        "k1": np.asarray(L0_ffn_k1).reshape(KH, P, KH, P).transpose(1, 2, 0, 3),
        "k2": np.asarray(L0_ffn_k2).reshape(KH, P, D).transpose(1, 0, 2),
        "s": np.stack([np.asarray(v).reshape(()) for v in (L0_ffn_s0, L0_ffn_s1, L0_ffn_s2)]).reshape(1, 3),
    }
    arrays = {f"in_{name}_dram": np.ascontiguousarray(a) for name, a in arrays.items()}

    nc = bacc.Bacc("TRN2", target_bir_lowering=False, num_devices=1)
    args = [nc.dram_tensor(name, a.shape, mybir.dt.from_np(a.dtype), kind="ExternalInput").ap()
            for name, a in arrays.items()]
    args.append(nc.dram_tensor("out_0_dram", (P, CHUNKS, KD, ROWS), mybir.dt.float32, kind="ExternalOutput").ap())
    build(nc, *args)
    r = run_bass_kernel_spmd(nc, [arrays], core_ids=[0])
    y = r.results[0]["out_0_dram"]
    return np.ascontiguousarray(y.transpose(1, 3, 2, 0).reshape(BATCH, SEQ, D))
```

```python
import concourse.bass as bass
from concourse import mybir
from contextlib import ExitStack

P = 128
BATCH, SEQ, D = 16, 256, 256
HID = 1024
EPS = 1e-8
ROWS = 512
CHUNKS = BATCH * SEQ // ROWS
PER = ROWS // SEQ
KD, KH = D // P, HID // P
WAKE = 9
RING = 4
WIDE = 2 * KH


def pieces(m, last):
    return [(0, 0, ROWS // 2), (1, ROWS // 2, ROWS)] if last and m == KD - 1 else [(0, 0, ROWS)]


def build(nc, x, wc, k0, k1, k2, s, out):
    fp32, fp32r, u8 = mybir.dt.float32, mybir.dt.float32r, mybir.dt.uint8
    ALU = mybir.AluOpType
    ACT = mybir.ActivationFunctionType

    ctx = ExitStack()
    with ctx:
        def sb(name, shape, dt=fp32):
            return ctx.enter_context(nc.sbuf_tensor(name, shape, dt))

        def banks(name, n):
            return [ctx.enter_context(nc.psum_tensor(f"{name}{i}", [P, ROWS], fp32)) for i in range(n)]

        def sem(name):
            return ctx.enter_context(nc.semaphore(name))

        x_sb = sb("x_sb", [P, CHUNKS, KD, ROWS])
        wc_sb = sb("wc_sb", [P, KD, D + BATCH])
        w_sb, cond_sb = wc_sb[:, :, 0:D], wc_sb[:, :, D:D + BATCH]
        s_sb = sb("s_sb", [P, 3])
        k0_sb = sb("k0_sb", [P, KH, 2, KD, P], u8)
        k1_sb = sb("k1_sb", [P, KH, KH, P], u8)
        k2_sb = sb("k2_sb", [P, KH, D], u8)
        ys = sb("ys", [P, KD, BATCH])
        ys2 = sb("ys2", [P, KD, BATCH])
        w2_sb = sb("w2_sb", [P, KD, D])
        var = sb("var", [P, KD, BATCH])
        root = sb("root", [P, KD, BATCH])
        rough = sb("rough", [P, KD, BATCH])
        step_a = sb("step_a", [P, KD, BATCH])
        step_b = sb("step_b", [P, KD, BATCH])
        demod = sb("demod", [P, KD, BATCH])
        idle = sb("idle", [P, ROWS], mybir.dt.bfloat16)
        gain = sb("gain", [P, 2])
        wt0 = sb("wt0", [P, KH, KD, P], fp32r)
        wt1 = sb("wt1", [P, KH, KH, P], fp32r)
        wt2 = sb("wt2", [P, KH, D], fp32r)
        xs = sb("xs", [P, 2, KD, ROWS])
        h0 = [sb(f"h0_{part}", [P, KD, ROWS], fp32r) for part in ("hi", "lo")]
        h1 = [sb(f"h1_{part}", [P, KH, ROWS], fp32r) for part in ("hi", "lo")]
        h2 = [sb(f"h2_{part}", [P, KH, ROWS], fp32r) for part in ("hi", "lo")]
        t_cond = sb("t_cond", [P, KD, ROWS])
        t_wide = sb("t_wide", [P, RING, ROWS])

        wide_ps = banks("wide_ps", RING)
        cond_ps = banks("cond_ps", KD)
        out_ps = banks("out_ps", KD)

        def cond_banks(slot):
            return out_ps if slot else cond_ps

        def bank(m, piece):
            return cond_ps[0] if piece else out_ps[m]


        wc_in, s_in = sem("wc_in"), sem("s_in")
        x0_in = [sem(f"x0_in{kt}") for kt in range(KD)]
        x_in = {c: sem(f"x_in{c}") for c in range(1, CHUNKS)}
        k0_in, k1_in, k2_in = [sem("k0_in0"), sem("k0_in1")], [sem("k1_in0"), sem("k1_in1")], sem("k2_in")
        idle_made, root_table = sem("idle_made"), sem("root_table")
        ys_made, setup_v = sem("ys_made"), sem("setup_v")
        squares_made = sem("squares_made")
        var_summed, var_made, root_made, demod_made = (
            sem("var_summed"), sem("var_made"), sem("root_made"), sem("demod_made"))
        gain_made = sem("gain_made")
        wt0_made, wt1_made, wt2_made = sem("wt0_made"), sem("wt1_made"), sem("wt2_made")
        xs0_made = sem("xs0_made")
        xs_made = sem("xs_made")
        cond_done = sem("cond_done")
        cond_scaled = sem("cond_scaled")
        cond_split = sem("cond_split")
        wide_done = sem("wide_done")
        wide_relu = sem("wide_relu")
        wide_split = sem("wide_split")
        hi_made = sem("hi_made")
        out_done = sem("out_done")
        y_made = sem("y_made")
        y_stored = sem("y_stored")

        block = ctx.enter_context(nc.Block())

        @block.sync
        def _(sp):
            sp.dma_start(wc_sb[:], wc).then_inc(wc_in, 16)
            for kt in range(KD):
                sp.dma_start(x_sb[:, 0, kt], x[:, 0, kt]).then_inc(x0_in[kt], 16)
            sp.dma_start(x_sb[:, 1], x[:, 1]).then_inc(x_in[1], 16)
            sp.dma_start(s_sb[:], s.to_broadcast([P, 3])).then_inc(s_in, 16)
            half = KH // 2
            for i in range(2):
                sp.dma_start(k0_sb[:, i * half:(i + 1) * half], k0[:, i * half:(i + 1) * half]).then_inc(k0_in[i], 16)
            for i in range(2):
                sp.dma_start(k1_sb[:, i * half:(i + 1) * half], k1[:, i * half:(i + 1) * half]).then_inc(k1_in[i], 16)
            sp.dma_start(k2_sb[:], k2).then_inc(k2_in, 16)
            for c in range(2, CHUNKS):
                sp.dma_start(x_sb[:, c], x[:, c]).then_inc(x_in[c], 16)

            def store(c, last=False):
                n = KD * c
                for m in range(KD):
                    for i, a, b in pieces(m, last):
                        n += 1
                        sp.wait_ge(y_made, n)
                        sp.dma_start(out[:, c, m, a:b], x_sb[:, c, m, a:b]).then_inc(y_stored, 16)
                return n

            with sp.Fori(0, CHUNKS - 1) as c:
                store(c)
            sp.wait_ge(y_stored, 16 * store(CHUNKS - 1, last=True))

        @block.gpsimd
        def _(pool):
            for m in range(KH):
                if m % (KH // 2) == 0:
                    pool.wait_ge(k1_in[m // (KH // 2)], 16)
                pool.tensor_scalar(wt1[:, m], k1_sb[:, m], 2.0, -1.0, ALU.mult, ALU.add).then_inc(wt1_made, 1)
            pool.wait_ge(k2_in, 16)
            pool.tensor_scalar(wt2[:], k2_sb[:], 2.0, -1.0, ALU.mult, ALU.add).then_inc(wt2_made, 1)

        @block.scalar
        def _(act):
            def modulate(c, slot=0):
                for kt in range(KD):
                    for b in range(PER):
                        last = act.activation(xs[:, slot, kt, b * SEQ:(b + 1) * SEQ], x_sb[:, c, kt, b * SEQ:(b + 1) * SEQ],
                                              ACT.Copy, scale=ys[:, kt, bass.ds(PER * c + b, 1)])
                last.then_inc(xs_made, 1)

            def scale_cond(c, first=False, slot=0):
                for m in range(KD):
                    act.wait_ge(cond_done, KD * c + m + 1)
                    if not first:
                        act.wait_ge(cond_split, KD * (c - 1) + m + 1)
                    for b in range(PER):
                        last = act.activation(t_cond[:, m, b * SEQ:(b + 1) * SEQ], cond_banks(slot)[m][:, b * SEQ:(b + 1) * SEQ],
                                              ACT.Copy, scale=demod[:, m, bass.ds(PER * c + b, 1)])
                    last.then_inc(cond_scaled, 1)

            def relu(c, layer, first=False):
                for m in range(KH):
                    n = WIDE * c + KH * layer + m
                    act.wait_ge(wide_done, n + 1)
                    if not (first and m < RING):
                        act.wait_ge(wide_split, n - RING + 1)
                    act.activation(t_wide[:, m % RING], wide_ps[m % RING][:], ACT.Relu,
                                   scale=gain[:, layer:layer + 1]).then_inc(wide_relu, 1)

            act.wait_ge(idle_made, 1)
            act.activation(root[:, 0, 0:1], idle[:, 0:1], ACT.Sqrt).then_inc(root_table, 1)
            act.wait_ge(ys_made, 1)
            act.wait_ge(x_in[1], 16)
            modulate(1, slot=1)
            act.wait_ge(var_made, 1)
            act.wait_ge(root_table, 1)
            act.activation(root[:], var[:], ACT.Sqrt).then_inc(root_made, 1)
            act.wait_ge(demod_made, 1)
            scale_cond(0, first=True)
            act.wait_ge(gain_made, 2)
            relu(0, 0, first=True)
            scale_cond(1, slot=1)
            act.wait_ge(x_in[2], 16)
            modulate(2)
            relu(0, 1)
            for c in range(3, CHUNKS):
                act.wait_ge(x_in[c], 16)
            with act.Fori(1, CHUNKS - 2) as c:
                relu(c, 0)
                scale_cond(c + 1)
                modulate(c + 2)
                relu(c, 1)
            relu(CHUNKS - 2, 0)
            scale_cond(CHUNKS - 1)
            relu(CHUNKS - 2, 1)
            relu(CHUNKS - 1, 0)
            relu(CHUNKS - 1, 1)

        @block.vector
        def _(dve):
            def high(t, h, m):
                dve.tensor_copy(h[0][:, m], t).then_inc(hi_made, 1)

            def low(t, h, m, count):
                dve.wait_ge(hi_made, count)
                return dve.tensor_tensor(h[1][:, m], t, h[0][:, m].bitcast(fp32), ALU.subtract)

            def before(c):
                return (WIDE + KD) * c + KD

            def split_cond(c, at):
                for m in range(KD):
                    dve.wait_ge(cond_scaled, KD * c + m + 1)
                    high(t_cond[:, m], h0, m)
                    low(t_cond[:, m], h0, m, at + m + 1).then_inc(cond_split, 1)

            def split_wide(c, layer, at):
                h = (h1, h2)[layer]
                for m in range(KH):
                    dve.wait_ge(wide_relu, WIDE * c + KH * layer + m + 1)
                    high(t_wide[:, m % RING], h, m)
                    if layer == 0 and m > 0:
                        low(t_wide[:, (m - 1) % RING], h, m - 1, at + m).then_inc(wide_split, 1)
                    if layer == 1 or m == KH - 1:
                        low(t_wide[:, m % RING], h, m, at + m + 1).then_inc(wide_split, 1)

            def finish(c, last=False):
                n = KD * c
                for m in range(KD):
                    for i, a, b in pieces(m, last):
                        n += 1
                        dve.wait_ge(out_done, n)
                        dve.scalar_tensor_tensor(x_sb[:, c, m, a:b], bank(m, i)[:, a:b], s_sb[:, 2:3],
                                                 x_sb[:, c, m, a:b], ALU.mult, ALU.add).then_inc(y_made, 1)

            def fold(m):
                if m % (KH // 2) == 0:
                    dve.wait_ge(k0_in[m // (KH // 2)], 16)
                dve.tensor_tensor(wt0[:, m], k0_sb[:, m, 0], k0_sb[:, m, 1], ALU.subtract).then_inc(wt0_made, 1)

            dve.memset(idle[:], 0.0).then_inc(idle_made, 1)
            dve.wait_ge(wc_in, 16)
            dve.tensor_scalar(ys[:], cond_sb, float(D) ** -0.5, None, ALU.mult).then_inc(ys_made, 1)
            dve.wait_ge(ys_made, 1)
            dve.tensor_tensor(ys2[:], ys[:], ys[:], ALU.mult).then_inc(squares_made, 1)
            for kt in range(KD):
                dve.tensor_tensor(w2_sb[:, kt], w_sb[:, kt], w_sb[:, kt], ALU.mult).then_inc(squares_made, 1)
            for kt in range(KD):
                dve.wait_ge(x0_in[kt], 16)
                for b in range(PER):
                    last = dve.tensor_scalar(xs[:, 0, kt, b * SEQ:(b + 1) * SEQ], x_sb[:, 0, kt, b * SEQ:(b + 1) * SEQ],
                                             ys[:, kt, b:b + 1], None, ALU.mult)
                last.then_inc(xs0_made, 1)
            dve.wait_ge(var_summed, 1)
            for m in range(KD):
                last = dve.tensor_scalar(var[:, m], wide_ps[m][:, 0:BATCH], EPS, None, ALU.add)
            last.then_inc(var_made, 1)
            fold(0)
            fold(1)
            dve.wait_ge(root_made, 1)
            dve.reciprocal(rough[:], root[:]).then_inc(setup_v, 1)
            dve.wait_ge(setup_v, 1)
            dve.scalar_tensor_tensor(step_a[:], rough[:], -0.5, var[:], ALU.mult, ALU.mult).then_inc(setup_v, 1)
            dve.wait_ge(setup_v, 2)
            dve.tensor_tensor(step_b[:], step_a[:], rough[:], ALU.mult).then_inc(setup_v, 1)
            dve.wait_ge(setup_v, 3)
            dve.scalar_tensor_tensor(demod[:], step_b[:], 1.5, rough[:], ALU.add, ALU.mult).then_inc(demod_made, 1)
            dve.wait_ge(s_in, 16)
            dve.tensor_scalar(gain[:, 0:1], s_sb[:, 0:1], 4.0, None, ALU.mult).then_inc(gain_made, 1)
            dve.tensor_scalar(gain[:, 1:2], s_sb[:, 1:2], 2.0, None, ALU.mult).then_inc(gain_made, 1)
            fold(2)
            fold(3)
            split_cond(0, 0)
            for m in range(4, KH):
                fold(m)
            split_wide(0, 0, before(0))
            split_cond(1, before(0) + KH)
            split_wide(0, 1, before(0) + KH + KD)
            with dve.Fori(1, CHUNKS - 1) as c:
                split_wide(c, 0, before(c))
                split_cond(c + 1, before(c) + KH)
                finish(c - 1)
                split_wide(c, 1, before(c) + KH + KD)
            c = CHUNKS - 1
            split_wide(c, 0, before(c))
            finish(c - 1)
            split_wide(c, 1, before(c) + KH)
            finish(c, last=True)

        @block.tensor
        def _(pe):
            def variance():
                for kt in range(KD):
                    pe.wait_ge(squares_made, kt + 2)
                    for m in range(KD):
                        mm = pe.matmul(wide_ps[m][:, 0:BATCH], w2_sb[:, kt, m * P:(m + 1) * P], ys2[:, kt],
                                       start=(kt == 0), stop=(kt == KD - 1))
                mm.then_inc(var_summed, 1)

            def project(c, first=False, slot=0):
                if not first:
                    pe.wait_ge(xs_made, c)
                for m in range(KD):
                    if not (first or slot):
                        pe.wait_ge(cond_scaled, KD * (c - 1) + m + 1)
                    for kt in range(KD):
                        if first and m == 0:
                            pe.wait_ge(xs0_made, kt + 1)
                        mm = pe.matmul(cond_banks(slot)[m][:], w_sb[:, kt, m * P:(m + 1) * P], xs[:, slot, kt],
                                       start=(kt == 0), stop=(kt == KD - 1))
                    mm.then_inc(cond_done, 1)
                    if first and m == 0:
                        variance()

            def layer1(c, first=False):
                for m in range(KH):
                    n = WIDE * c + m
                    if first:
                        pe.wait_ge(wt0_made, m + 1)
                    if not (first and m < RING):
                        pe.wait_ge(wide_relu, n - RING + 1)
                    for kt in range(KD):
                        if m == 0:
                            pe.wait_ge(cond_split, KD * c + kt + 1)
                        for part in range(2):
                            mm = pe.matmul(wide_ps[m % RING][:], wt0[:, m, kt], h0[part][:, kt],
                                           start=(kt == 0 and part == 0), stop=(kt == KD - 1 and part == 1))
                    mm.then_inc(wide_done, 1)

            def layer2(c, first=False):
                for m in range(KH):
                    n = WIDE * c + KH + m
                    if first:
                        pe.wait_ge(wt1_made, m + 1)
                    pe.wait_ge(wide_relu, n - RING + 1)
                    for kt in range(KH):
                        if m == 0:
                            pe.wait_ge(wide_split, WIDE * c + kt + 1)
                        for part in range(2):
                            mm = pe.matmul(wide_ps[m % RING][:], wt1[:, m, kt], h1[part][:, kt],
                                           start=(kt == 0 and part == 0), stop=(kt == KH - 1 and part == 1))
                    mm.then_inc(wide_done, 1)

            def layer3(c, first=False, last=False):
                if first:
                    pe.wait_ge(wt2_made, 1)
                else:
                    pe.wait_ge(y_made, KD * c)
                for m in range(KD):
                    for i, a, b in pieces(m, last):
                        for kt in range(KH):
                            if m == 0:
                                pe.wait_ge(wide_split, WIDE * c + KH + kt + 1)
                            for part in range(2):
                                mm = pe.matmul(bank(m, i)[:, a:b], wt2[:, kt, m * P:(m + 1) * P],
                                               h2[part][:, kt, a:b],
                                               start=(kt == 0 and part == 0), stop=(kt == KH - 1 and part == 1))
                        mm.then_inc(out_done, 1)

            pe.wait_ge(idle_made, 1)
            for i in range(WAKE):
                pe.matmul(wide_ps[0][:], idle[:, 0:P], idle[:], start=True, stop=True)
            project(0, first=True)
            project(1, slot=1)
            layer1(0, first=True)
            layer2(0, first=True)
            layer1(1)
            project(2)
            layer3(0, first=True)
            layer2(1)
            with pe.Fori(2, CHUNKS - 1) as c:
                layer1(c)
                project(c + 1)
                layer3(c - 1)
                layer2(c)
            layer1(CHUNKS - 1)
            layer3(CHUNKS - 2)
            layer2(CHUNKS - 1)
            layer3(CHUNKS - 1, last=True)


def kernel(x, cond_1024, L0_cond_weight, L0_ffn_k0, L0_ffn_k1, L0_ffn_k2, L0_ffn_s0, L0_ffn_s1, L0_ffn_s2):
    import numpy as np
    import concourse.bacc as bacc
    from concourse.bass_utils import run_bass_kernel_spmd

    arrays = {
        "x": np.asarray(x).reshape(CHUNKS, ROWS, KD, P).transpose(3, 0, 2, 1),
        "wc": np.concatenate([np.asarray(L0_cond_weight).reshape(KD, P, D).transpose(1, 0, 2),
                              np.asarray(cond_1024).reshape(BATCH, KD, P).transpose(2, 1, 0)], axis=2),
        "k0": np.asarray(L0_ffn_k0).reshape(2, KD, P, KH, P).transpose(2, 3, 0, 1, 4),
        "k1": np.asarray(L0_ffn_k1).reshape(KH, P, KH, P).transpose(1, 2, 0, 3),
        "k2": np.asarray(L0_ffn_k2).reshape(KH, P, D).transpose(1, 0, 2),
        "s": np.stack([np.asarray(v).reshape(()) for v in (L0_ffn_s0, L0_ffn_s1, L0_ffn_s2)]).reshape(1, 3),
    }
    arrays = {f"in_{name}_dram": np.ascontiguousarray(a) for name, a in arrays.items()}

    nc = bacc.Bacc("TRN2", target_bir_lowering=False, num_devices=1)
    args = [nc.dram_tensor(name, a.shape, mybir.dt.from_np(a.dtype), kind="ExternalInput").ap()
            for name, a in arrays.items()]
    args.append(nc.dram_tensor("out_0_dram", (P, CHUNKS, KD, ROWS), mybir.dt.float32, kind="ExternalOutput").ap())
    build(nc, *args)
    r = run_bass_kernel_spmd(nc, [arrays], core_ids=[0])
    y = r.results[0]["out_0_dram"]
    return np.ascontiguousarray(y.transpose(1, 3, 2, 0).reshape(BATCH, SEQ, D))
```
